# Optimizing a Trainium2 kernel written in Bass

```python
import numpy as np
import jax
import jax.numpy as jnp

def _softmax(x, axis=-1):
    return jax.nn.softmax(x, axis=axis)
def _gelu(x):
    return jax.nn.gelu(x, approximate=True)
def _silu(x):
    return jax.nn.silu(x)
def _sigmoid(x):
    return jax.nn.sigmoid(x)
def _layernorm(x, axis=-1, eps=1e-5):
    m = jnp.mean(x, axis=axis, keepdims=True)
    v = jnp.var(x, axis=axis, keepdims=True)
    return (x - m) / jnp.sqrt(v + eps)
def _scatter_add(tgt, idx, src, axis=0):
    return tgt.at[idx].add(src)
def _segment_sum(src, seg, n):
    return jax.ops.segment_sum(src, seg, n)

kernel_name = 'mk_conv_preact_d1_conv_nchw384_6276e6'

def setup_inputs(seed: int = 0):
    np.random.seed(seed)
    _w = jnp.asarray
    def _rec_inputs():
        import jax
        import jax.numpy as jnp
        _gk = jax.random.key(seed)
        x = -0.0001476 + 0.9999 * jax.random.normal(jax.random.fold_in(_gk, 1), (32, 384, 56, 56), jnp.float32)
        return x
    x = _rec_inputs()
    def _L0_conv_setup():
        import jax, jax.numpy as jnp
        import numpy as np
        C = 384

        def dwconv(x, w, pad_h, pad_w, stride=(1, 1)):
            return jax.lax.conv_general_dilated(x, w, window_strides=stride, padding=((pad_h, pad_h), (pad_w, pad_w)), dimension_numbers=('NCHW', 'OIHW', 'NCHW'), feature_group_count=C)
        key = jax.random.key(seed)
        ks = jax.random.split(key, 12)
        f = lambda k, shape: jax.random.normal(k, shape, dtype=jnp.float32) * 0.05
        return {'x': jax.random.normal(ks[0], (32, C, 56, 56), dtype=jnp.float32), 'w77': f(ks[1], (C, 1, 7, 7)), 'b77': f(ks[2], (C,)), 'w53': f(ks[3], (C, 1, 5, 3)), 'b53': f(ks[4], (C,)), 'w35': f(ks[5], (C, 1, 3, 5)), 'b35': f(ks[6], (C,)), 'w7w': f(ks[7], (C, 1, 1, 7)), 'w7h': f(ks[8], (C, 1, 7, 1)), 'w5w': f(ks[9], (C, 1, 1, 5)), 'w5h': f(ks[10], (C, 1, 5, 1))}
    _L0_conv_all = _L0_conv_setup()
    _L0_conv_in = {k: v for k, v in _L0_conv_all.items() if k in ('w77', 'b77', 'w53', 'b53', 'w35', 'b35', 'w7w', 'w7h', 'w5w', 'w5h', )}
    del _L0_conv_all

    return {
        "x": x,
        "L0_conv_w77": _L0_conv_in["w77"],
        "L0_conv_b77": _L0_conv_in["b77"],
        "L0_conv_w53": _L0_conv_in["w53"],
        "L0_conv_b53": _L0_conv_in["b53"],
        "L0_conv_w35": _L0_conv_in["w35"],
        "L0_conv_b35": _L0_conv_in["b35"],
        "L0_conv_w7w": _L0_conv_in["w7w"],
        "L0_conv_w7h": _L0_conv_in["w7h"],
        "L0_conv_w5w": _L0_conv_in["w5w"],
        "L0_conv_w5h": _L0_conv_in["w5h"],
    }

def reference(x, L0_conv_w77, L0_conv_b77, L0_conv_w53, L0_conv_b53, L0_conv_w35, L0_conv_b35, L0_conv_w7w, L0_conv_w7h, L0_conv_w5w, L0_conv_w5h):
    import jax
    import jax.numpy as jnp
    def _L0_conv_ref(x, w77, b77, w53, b53, w35, b35, w7w, w7h, w5w, w5h):
        import jax, jax.numpy as jnp
        import numpy as np
        C = 384

        def dwconv(x, w, pad_h, pad_w, stride=(1, 1)):
            return jax.lax.conv_general_dilated(x, w, window_strides=stride, padding=((pad_h, pad_h), (pad_w, pad_w)), dimension_numbers=('NCHW', 'OIHW', 'NCHW'), feature_group_count=C)
        bias = (b77 + b53 + b35)[None, :, None, None]
        out = dwconv(x, w77, 3, 3) + dwconv(x, w53, 2, 1) + dwconv(x, w35, 1, 2) + dwconv(dwconv(x, w7w, 0, 3), w7h, 3, 0) + dwconv(dwconv(x, w5w, 0, 2), w5h, 2, 0) + bias
        return out

    def _gn(v, G=32, eps=1e-5):
        B_, C_, H_, W_ = v.shape
        g = v.reshape(B_, G, C_ // G, H_, W_)
        m = jnp.mean(g, axis=(2, 3, 4), keepdims=True)
        s = jnp.var(g, axis=(2, 3, 4), keepdims=True)
        return ((g - m) / jnp.sqrt(s + eps)).reshape(v.shape)

    def _ln_c(v, eps=1e-6):
        m = jnp.mean(v, axis=1, keepdims=True)
        s = jnp.var(v, axis=1, keepdims=True)
        return (v - m) / jnp.sqrt(s + eps)

    def _ln_t(v, eps=1e-5):
        m = jnp.mean(v, axis=-1, keepdims=True)
        s = jnp.var(v, axis=-1, keepdims=True)
        return (v - m) / jnp.sqrt(s + eps)

    def _to_tokens(v):
        B_, C_, H_, W_ = v.shape
        return v.reshape(B_, C_, H_ * W_).transpose(0, 2, 1)
    def _from_tokens(t, like):
        B_, C_, H_, W_ = like.shape
        return t.transpose(0, 2, 1).reshape(B_, C_, H_, W_)

    x = x + _L0_conv_ref(_gn(x), L0_conv_w77, L0_conv_b77, L0_conv_w53, L0_conv_b53, L0_conv_w35, L0_conv_b35, L0_conv_w7w, L0_conv_w7h, L0_conv_w5w, L0_conv_w5h)
    return x


_drawn_inputs = setup_inputs


def setup_inputs(seed=0):
    import zlib

    import numpy as np

    out = dict(_drawn_inputs(seed))
    spreads = {}
    factors = {'L0_conv_w7w': 3.654, 'L0_conv_w7h': 3.761, 'L0_conv_w5w': 4.756, 'L0_conv_w5h': 4.898}
    for name, (base, spread) in spreads.items():
        noise = np.random.default_rng([zlib.crc32(name.encode()), seed]).standard_normal(out[name].shape)
        drawn = base * np.exp(spread * noise) if base else spread * noise
        out[name] = jnp.asarray(drawn.astype(out[name].dtype))
    for name, factor in factors.items():
        out[name] = (out[name] * factor).astype(out[name].dtype)
    return out
```

```python
import concourse.bass as bass
from concourse import mybir
from contextlib import ExitStack


def bass_groupnorm_dwconv_kernel(nc: bass.Bass, x, w77, b77, w53, b53, w35, b35, w7w, w7h, w5w, w5h, out):
    fp32 = mybir.dt.float32
    fp16 = mybir.dt.float16
    ALU = mybir.AluOpType
    ACT = mybir.ActivationFunctionType
    AX = mybir.AxisListType

    B, C, H, W = x.shape
    P = 128
    GROUPS = 32
    CG = C // GROUPS
    Q = P // B
    ROWS = H // Q
    PIX = ROWS * W
    TW = 8
    NT = W // TW
    KP = ROWS * TW
    PAD = 3
    TAPS = 2 * PAD + 1
    OW = TW + 2 * PAD
    OR = ROWS + 2 * PAD
    BAND = OR * OW
    HALF = ROWS // 2
    BANK = 512
    TS = P + B
    CB = C // P

    CHUNK = 4
    NCH = CG // CHUNK
    LOAD_AT = (3, 5, 7)
    XRING = 3
    STAT = 448
    NSTAT = CG * PIX // STAT
    STAT_SLOTS = 7
    PER_SLOT = NSTAT // STAT_SLOTS
    EPS = 1e-5
    XSCALE = 256.0
    KSCALE = 16384.0
    STRIP = 512
    FIRST_TAP = (OR - 4) * OW + (OW - 4) - PAD * OW - PAD

    taps_strip = nc.dram_tensor("taps_strip", [C, 2, STRIP], fp16, kind="Internal").ap()
    chan_dram = nc.dram_tensor("chan_dram", [2, C], fp32, kind="Internal").ap()
    stats_dram = nc.dram_tensor("stats_dram", [P, 3], fp32, kind="Internal").ap()

    ctx = ExitStack()
    with ctx:
        def sb(name, shape, dt):
            return ctx.enter_context(nc.sbuf_tensor(name, shape, dt))

        def sem(name):
            return ctx.enter_context(nc.semaphore(name))

        xin = sb("xin", [P, XRING, CG, PIX], fp32)
        xnorm = sb("xnorm", [P, 3, PIX], fp32)
        xT = sb("xT", [KP, 2, 2, NT * TS + B], fp16)
        band = sb("band", [KP, CG, 2, BAND], fp16)
        y = sb("y", [P, 2, PIX], fp32)
        chan = sb("chan", [P, 2, C], fp32)
        norm = sb("norm", [P, 2, 2], fp32)
        bns = sb("bns", [P, NSTAT, 6], fp32)
        triple = sb("triple", [P, 3], fp32)
        quad = sb("quad", [P, Q, 3], fp32)
        mv = sb("mv", [P, 2], fp32)
        tmp = sb("tmp", [P, 4], fp32)
        root = sb("root", [P, 1], fp32)
        pace = sb("pace", [P, 1], fp32)
        ident = sb("ident", [P, P], fp32)
        k77 = sb("k77", [P, CB, TAPS, TAPS], fp32)
        k53 = sb("k53", [P, CB, 5, 3], fp32)
        k35 = sb("k35", [P, CB, 3, 5], fp32)
        k7w = sb("k7w", [P, CB, 7], fp32)
        k7h = sb("k7h", [P, CB, 7], fp32)
        k5w = sb("k5w", [P, CB, 5], fp32)
        k5h = sb("k5h", [P, CB, 5], fp32)
        bia = sb("bia", [P, 3, CB], fp32)
        outer7 = sb("outer7", [P, CB, 7, 7], fp32)
        outer5 = sb("outer5", [P, CB, 5, 5], fp32)
        kabs = sb("kabs", [P, CB, TAPS * TAPS], fp32)
        kmax = sb("kmax", [P, CB], fp32)
        krec = sb("krec", [P, CB], fp32)
        chcol = sb("chcol", [P, 2, CB], fp32)
        strip = sb("strip", [P, CB, 2, STRIP], fp16)

        tps = ctx.enter_context(nc.psum_tensor("tps", [P, 2, 2 * BANK], fp32))
        cps = ctx.enter_context(nc.psum_tensor("cps", [P, 2, 2, BANK], fp32))

        weights_loaded = sem("weights_loaded")
        strip_zeroed = sem("strip_zeroed")
        ident_zeroed = sem("ident_zeroed")
        ident_ready = sem("ident_ready")
        setup_step = sem("setup_step")
        strip_ready = sem("strip_ready")
        chcol_ready = sem("chcol_ready")
        strip_saved = sem("strip_saved")
        chan_saved = sem("chan_saved")
        chan_loaded = sem("chan_loaded")
        x_loaded = [sem(f"x_loaded{k}") for k in range(NCH)]
        x_stored = [sem(f"x_stored{k}") for k in range(NCH)]
        band_loaded = [sem(f"band_loaded{k}") for k in range(NCH)]
        triple_ready = sem("triple_ready")
        triple_saved = sem("triple_saved")
        quad_loaded = sem("quad_loaded")
        stat_step = sem("stat_step")
        var_ready = sem("var_ready")
        root_ready = sem("root_ready")
        norm_ready = sem("norm_ready")
        xnorm_ready = sem("xnorm_ready")
        transposed = sem("transposed")
        lo_ready = sem("lo_ready")
        conv_done = sem("conv_done")
        y_ready = sem("y_ready")
        sum_done = sem("sum_done")
        hi_ready = sem("hi_ready")

        N_STAT_STEPS = 8

        def x_block(dram, g, k, q):
            return bass.AP(dram.tensor, (g * CG + k * CHUNK) * H * W + q * PIX,
                           [[C * H * W, B], [H * W, CHUNK], [1, PIX]])

        def x_slot(g, k, q):
            return xin[q * B:(q + 1) * B, bass.ds(g % XRING, 1), k * CHUNK:(k + 1) * CHUNK, :]

        block = ctx.enter_context(nc.Block())

        @block.sync
        def _(sp):
            small = [(k77[:, :, :, :], w77, 49), (k53[:, :, :, :], w53, 15), (k35[:, :, :, :], w35, 15),
                     (k7w[:, :, :], w7w, 7), (k7h[:, :, :], w7h, 7), (k5w[:, :, :], w5w, 5), (k5h[:, :, :], w5h, 5),
                     (bia[:, 0, :], b77, 1), (bia[:, 1, :], b53, 1), (bia[:, 2, :], b35, 1)]
            for dst, src, n in small:
                sp.dma_start(dst, bass.AP(src.tensor, 0, [[CB * n, P], [1, CB * n]])).then_inc(weights_loaded, 16)
            sp.wait_ge(strip_ready, 1)
            sp.dma_start(bass.AP(taps_strip.tensor, 0, [[CB * 2 * STRIP, P], [1, CB * 2 * STRIP]]),
                         strip[:, :, :, :]).then_inc(strip_saved, 16)

            def load_band(g, k):
                for w in range(TW):
                    sp.dma_start(band[w:w + TW * (ROWS - 1) + 1:TW, k * CHUNK:(k + 1) * CHUNK, :, :],
                                 bass.AP(taps_strip.tensor, (g * CG + k * CHUNK) * 2 * STRIP + w,
                                         [[OW, ROWS], [STRIP, 2 * CHUNK], [1, BAND]])).then_inc(band_loaded[k], 16)

            def store(g, k):
                sp.wait_ge(sum_done, g * CG + (k + 1) * CHUNK + 2)
                for q in (0, 2, 1, 3):
                    sp.dma_start(x_block(out, g, k, q), x_slot(g, k, q)).then_inc(x_stored[k], 16)

            sp.wait_ge(strip_saved, 16)
            for k in range(NCH):
                load_band(0, k)
            def steps(g, first):
                for k in range(NCH):
                    sp.wait_ge(conv_done, g * CG + (k + 1) * CHUNK + 2)
                    sp.wait_ge(band_loaded[k], (g + 1) * (16 * TW))
                    load_band(g + 1, k)
                    if not first:
                        sp.wait_ge(x_stored[k], g * (16 * Q))
                    store(g, k)

            steps(0, True)
            with sp.Fori(1, GROUPS - 1) as g:
                steps(g, False)
            for k in range(NCH):
                sp.wait_ge(x_stored[k], (GROUPS - 1) * (16 * Q))
                store(GROUPS - 1, k)
            for k in range(NCH):
                sp.wait_ge(x_stored[k], GROUPS * (16 * Q))

        @block.gpsimd
        def _(pool):
            nc.gpsimd.memset(ident[:, :], 0.0).then_inc(ident_zeroed, 1)
            nc.gpsimd.memset(strip[:, :, :, :], 0.0).then_inc(strip_zeroed, 1)
            pool.wait_ge(ident_zeroed, 1)
            nc.gpsimd.affine_select(out=ident[:, :], in_=ident[:, :], compare_op=ALU.not_equal, fill=1.0,
                                    base=0, pattern=[[-1, P]], channel_multiplier=1).then_inc(ident_ready, 1)
            nc.gpsimd.memset(xT[:, :, :, :], 0.0).then_inc(conv_done, 2)
            pool.wait_ge(conv_done, 2)
            nc.gpsimd.memset(y[:, 0, 0:1], 0.0).then_inc(sum_done, 2)
            with pool.Fori(0, GROUPS) as g:
                for i in range(CG):
                    pool.wait_ge(y_ready, g * CG + i + 3)
                    xs = xin[:, bass.ds(g % XRING, 1), i, :].rearrange("p a n -> p (a n)")
                    nc.gpsimd.tensor_tensor(xs, xs, y[:, i % 2, :], ALU.add).then_inc(sum_done, 1)

        @block.scalar
        def _(act):
            def load(g, k):
                for q in (0, 2, 1, 3):
                    act.dma_start(x_slot(g, k, q), x_block(x, g, k, q)).then_inc(x_loaded[k], 16)

            def normalise(g, i, slot):
                xs = xin[:, bass.ds(g % XRING, 1), i, :].rearrange("p a (h t w) -> p (a h) t w", h=ROWS, w=TW)
                nrm = norm[:, bass.ds(g % 2, 1), :].rearrange("p a n -> p (a n)")
                tiles = xnorm[:, slot, ::-1].rearrange("p (t h w) -> p h t w", h=ROWS, w=TW)
                nc.scalar.activation(tiles, xs, ACT.Identity, bias=nrm[:, 1:2],
                                     scale=nrm[:, 0:1]).then_inc(xnorm_ready, 1)

            def high(slot):
                dst = xT[:, slot, 0, B:].rearrange("p (t c) -> p t c", c=TS)[:, :, 0:P]
                src = tps[0:KP, slot, 0:NT * P].rearrange("p (t c) -> p t c", c=P)
                nc.scalar.activation(dst, src, ACT.Copy).then_inc(hi_ready, 1)

            for g in range(2):
                for k in range(NCH):
                    if g:
                        act.wait_ge(x_loaded[k], 16 * Q)
                    load(g, k)
            act.wait_ge(chcol_ready, 1)
            act.dma_start(bass.AP(chan_dram.tensor, 0, [[CB, P], [C, 2], [1, CB]]), chcol[:, :, :]).then_inc(chan_saved, 16)

            def share_triples():
                act.dma_start(stats_dram[:, :], triple[:, :]).then_inc(triple_saved, 16)

            def fetch_quads():
                for q in range(Q):
                    act.dma_start(quad[q * B:(q + 1) * B, :, :],
                                  bass.AP(stats_dram.tensor, 0, [[3, B], [3 * B, Q], [1, 3]])).then_inc(quad_loaded, 16)

            def standard_deviation(g):
                act.wait_ge(var_ready, g + 1)
                nc.scalar.activation(root[:, :], tmp[:, 0:1], ACT.Sqrt).then_inc(root_ready, 1)

            act.wait_ge(triple_ready, 1)
            share_triples()
            act.wait_ge(triple_saved, 16)
            fetch_quads()
            act.wait_ge(chan_saved, 16)
            act.dma_start(chan[:, :, :], bass.AP(chan_dram.tensor, 0, [[0, P], [1, 2 * C]])).then_inc(chan_loaded, 16)
            standard_deviation(0)
            act.wait_ge(norm_ready, 1)
            act.wait_ge(transposed, 3)
            normalise(0, 0, 0)
            normalise(0, 1, 1)
            act.wait_ge(transposed, 4)
            act.wait_ge(conv_done, 2)
            high(0)
            act.wait_ge(chan_loaded, 16)

            def load_ahead(g, k, first):
                if not first:
                    act.wait_ge(x_stored[k], g * (16 * Q))
                act.wait_ge(x_loaded[k], (g + 2) * (16 * Q))
                load(g + 2, k)

            def steps(g, first, last):
                for i in range(CG):
                    n = g * CG + i
                    if i in LOAD_AT and not (type(g) is int and g + 2 >= GROUPS):
                        load_ahead(g, LOAD_AT.index(i), first)
                    if i + 1 < CG or not last:
                        act.wait_ge(transposed, n + 5)
                        act.wait_ge(conv_done, n + 2)
                        high((i + 1) % 2)
                    if i + 2 < CG or not last:
                        act.wait_ge(transposed, n + 3)
                        if i + 2 < CG:
                            normalise(g, i + 2, (i + 2) % 3)
                        else:
                            act.wait_ge(norm_ready, g + 2)
                            normalise(g + 1, i + 2 - CG, (i + 2) % 3)
                    if not last and i == STAT_SLOTS:
                        act.wait_ge(triple_ready, g + 2)
                        share_triples()
                    if not last and i == STAT_SLOTS + 1:
                        act.wait_ge(triple_saved, (g + 2) * 16)
                        fetch_quads()
                    act.wait_ge(conv_done, n + 3)
                    act.wait_ge(sum_done, n + 1)
                    nc.scalar.activation(y[:, i % 2, :].rearrange("p (a n) -> p a n", a=2),
                                         cps[:, i % 2, :, 0:HALF * W], ACT.Identity,
                                         bias=chan[:, 1, bass.ds(n, 1)],
                                         scale=chan[:, 0, bass.ds(n, 1)]).then_inc(y_ready, 1)
                    if not last and i == STAT_SLOTS + 2:
                        standard_deviation(g + 1)

            steps(0, True, False)
            with act.Fori(1, GROUPS - 2) as g:
                steps(g, False, False)
            steps(GROUPS - 2, False, False)
            steps(GROUPS - 1, False, True)

        @block.vector
        def _(dve):
            done = [0]

            def link(ins):
                done[0] += 1
                ins.then_inc(setup_step, 1)
                dve.wait_ge(setup_step, done[0])

            nc.vector.memset(tmp[:, 0:1], 0.0).then_inc(lo_ready, 2)
            nc.vector.memset(tmp[:, 1:2], 0.0).then_inc(y_ready, 2)
            nc.vector.memset(tmp[:, 2:3], 0.0).then_inc(transposed, 3)
            link(nc.vector.memset(triple[:, 0:1], 1.0))

            dve.wait_ge(weights_loaded, 160)
            nc.vector.tensor_tensor(outer7[:, :, :, :], k7h[:, :, :].unsqueeze(3).to_broadcast([P, CB, 7, 7]),
                                    k7w[:, :, :].unsqueeze(2).to_broadcast([P, CB, 7, 7]), ALU.mult)
            link(nc.vector.tensor_tensor(outer5[:, :, :, :], k5h[:, :, :].unsqueeze(3).to_broadcast([P, CB, 5, 5]),
                                         k5w[:, :, :].unsqueeze(2).to_broadcast([P, CB, 5, 5]), ALU.mult))
            link(nc.vector.tensor_tensor(k77[:, :, 1:6, 2:5], k77[:, :, 1:6, 2:5], k53[:, :, :, :], ALU.add))
            link(nc.vector.tensor_tensor(k77[:, :, 2:5, 1:6], k77[:, :, 2:5, 1:6], k35[:, :, :, :], ALU.add))
            link(nc.vector.tensor_tensor(k77[:, :, :, :], k77[:, :, :, :], outer7[:, :, :, :], ALU.add))
            link(nc.vector.tensor_tensor(k77[:, :, 1:6, 1:6], k77[:, :, 1:6, 1:6], outer5[:, :, :, :], ALU.add))
            flat = k77[:, :, :, :].rearrange("p c a b -> p c (a b)")
            link(nc.vector.scalar_tensor_tensor(out=kabs[:, :, :], in0=flat, scalar=-1.0, in1=flat, op0=ALU.mult, op1=ALU.max))
            link(nc.vector.tensor_reduce(kmax[:, :], kabs[:, :, :], AX.X, ALU.max))
            link(nc.vector.tensor_scalar(kmax[:, :], kmax[:, :], 1e-30, None, ALU.max))
            link(nc.vector.reciprocal(krec[:, :], kmax[:, :]))
            link(nc.vector.tensor_scalar(krec[:, :], krec[:, :], KSCALE, None, ALU.mult))
            link(nc.vector.tensor_tensor(kabs[:, :, :], flat, krec[:, :].unsqueeze(2).to_broadcast([P, CB, 49]), ALU.mult))
            dve.wait_ge(strip_zeroed, 1)
            hi, lo = [strip[:, :, part, FIRST_TAP:FIRST_TAP + TAPS * OW].rearrange("p c (a b) -> p c a b", b=OW)[:, :, :, 0:TAPS]
                      for part in range(2)]
            scaled = kabs[:, :, :].rearrange("p c (a b) -> p c a b", b=TAPS)
            link(nc.vector.tensor_copy(hi, scaled))
            nc.vector.tensor_tensor(lo, scaled, hi, ALU.subtract).then_inc(strip_ready, 1)
            nc.vector.tensor_scalar(chcol[:, 0, :], kmax[:, :], 1.0 / (KSCALE * XSCALE), None, ALU.mult)
            link(nc.vector.tensor_tensor(bia[:, 0, :], bia[:, 0, :], bia[:, 1, :], ALU.add))
            nc.vector.tensor_tensor(chcol[:, 1, :], bia[:, 0, :], bia[:, 2, :], ALU.add).then_inc(chcol_ready, 1)

            def statistics(g, s):
                if s * STAT % (CHUNK * PIX) == 0:
                    dve.wait_ge(x_loaded[s * STAT // (CHUNK * PIX)], (g + 1) * (16 * Q))
                xg = xin[:, bass.ds(g % XRING, 1), :, :].rearrange("p a c n -> p (a c n)")
                return nc.vector.bn_stats(bns[:, s, :], xg[:, s * STAT:(s + 1) * STAT])

            def aggregate(g):
                dve.wait_ge(stat_step, N_STAT_STEPS * g + 1)
                nc.vector.memset(pace[:, :], 0.0)
                nc.vector.bn_aggr(triple[:, 1:3], bns[:, :, :].rearrange("p s v -> p (s v)")).then_inc(triple_ready, 1)

            ve, r0, u = tmp[:, 0:1], tmp[:, 1:2], tmp[:, 2:3]

            def variance(g):
                dve.wait_ge(quad_loaded, (g + 1) * (16 * Q))
                nc.vector.memset(pace[:, :], 0.0)
                nc.vector.bn_aggr(mv[:, :], quad[:, :, :].rearrange("p q v -> p (q v)")).then_inc(stat_step, 1)
                dve.wait_ge(stat_step, N_STAT_STEPS * g + 2)
                nc.vector.tensor_scalar(ve, mv[:, 1:2], EPS, None, ALU.add).then_inc(var_ready, 1)

            def finish_norm(g):
                step = N_STAT_STEPS * g + 2
                nrm = norm[:, bass.ds(g % 2, 1), :].rearrange("p a n -> p (a n)")
                dve.wait_ge(root_ready, g + 1)
                nc.vector.reciprocal(r0, root[:, :]).then_inc(stat_step, 1)
                dve.wait_ge(stat_step, step + 1)
                nc.vector.tensor_tensor(u, r0, r0, ALU.mult).then_inc(stat_step, 1)
                dve.wait_ge(stat_step, step + 2)
                nc.vector.tensor_tensor(u, u, ve, ALU.mult).then_inc(stat_step, 1)
                dve.wait_ge(stat_step, step + 3)
                nc.vector.tensor_scalar(u, u, -0.5 * XSCALE, 1.5 * XSCALE, ALU.mult, ALU.add).then_inc(stat_step, 1)
                dve.wait_ge(stat_step, step + 4)
                nc.vector.tensor_tensor(nrm[:, 0:1], r0, u, ALU.mult).then_inc(stat_step, 1)
                dve.wait_ge(stat_step, step + 5)
                nc.vector.tensor_tensor(u, mv[:, 0:1], nrm[:, 0:1], ALU.mult).then_inc(stat_step, 1)
                dve.wait_ge(stat_step, step + 6)
                nc.vector.tensor_scalar(nrm[:, 1:2], u, -1.0, None, ALU.mult).then_inc(norm_ready, 1)

            def low(n, slot):
                dve.wait_ge(hi_ready, n + 1)
                hi = xT[:, slot, 0, B:].rearrange("p (t c) -> p t c", c=TS)[:, :, 0:P]
                lo = xT[:, slot, 1, B:].rearrange("p (t c) -> p t c", c=TS)[:, :, 0:P]
                src = tps[0:KP, slot, 0:NT * P].rearrange("p (t c) -> p t c", c=P)
                nc.vector.tensor_tensor(lo, src, hi, ALU.subtract).then_inc(lo_ready, 1)

            for s in range(NSTAT):
                last = statistics(0, s)
            last.then_inc(stat_step, 1)
            aggregate(0)
            variance(0)
            finish_norm(0)
            low(0, 0)

            def steps(g, last_group):
                for i in range(CG):
                    if not last_group and i == STAT_SLOTS + 3:
                        finish_norm(g + 1)
                    if i + 1 < CG or not last_group:
                        low(g * CG + i + 1, (i + 1) % 2)
                    if not last_group:
                        if i < STAT_SLOTS:
                            if i == 0:
                                dve.wait_ge(triple_ready, g + 1)
                            for s in range(i * PER_SLOT, (i + 1) * PER_SLOT):
                                last = statistics(g + 1, s)
                            if i == STAT_SLOTS - 1:
                                last.then_inc(stat_step, 1)
                                dve.wait_ge(triple_saved, (g + 1) * 16)
                                aggregate(g + 1)
                        if i == STAT_SLOTS + 2:
                            variance(g + 1)

            with dve.Fori(0, GROUPS - 1) as g:
                steps(g, False)
            steps(GROUPS - 1, True)

        @block.tensor
        def _(pe):
            def transpose(n, xslot, slot):
                pe.wait_ge(xnorm_ready, n + 1)
                pe.wait_ge(lo_ready, n + 1)
                for t in range(NT):
                    last = nc.tensor.transpose(tps[0:KP, slot, t * P:(t + 1) * P],
                                               xnorm[:, xslot, t * KP:(t + 1) * KP], ident[:, :])
                last.then_inc(transposed, 1)

            def convolve(n, i):
                slot = i % 2
                pe.wait_ge(lo_ready, n + 3)
                pe.wait_ge(y_ready, n + 1)
                mats = [band[:, i, part, :].rearrange("p (h w) -> p h w", w=OW) for part in range(2)]
                todo = []
                for t in range(NT):
                    w0 = W - (t + 1) * TW
                    lo = max(w0 - PAD, 0)
                    n_w = min(w0 + TW + PAD, W) - lo
                    off = lo - (w0 - PAD)
                    pieces = [(0, HALF, PAD, B), (HALF, HALF, PAD + HALF, B),
                              (0, PAD, PAD + ROWS, 0), (ROWS - PAD, PAD, 0, 2 * B)]
                    for xpart, kparts in ((0, (0, 1)), (1, (0,))):
                        for ho, rows, mrow, shift in pieces:
                            half, r = divmod(ho, HALF)
                            dst = cps[:, slot, half, 0:HALF * W].rearrange("p (h w) -> p h w", w=W)[:, r:r + rows, lo:lo + n_w]
                            for kpart in kparts:
                                todo.append((half, dst, xT[:, slot, xpart, t * TS + shift:t * TS + shift + P],
                                             mats[kpart][:, mrow:mrow + rows, off:off + n_w]))
                first = [next(j for j, m in enumerate(todo) if m[0] == half) for half in range(2)]
                final = [max(j for j, m in enumerate(todo) if m[0] == half) for half in range(2)]
                for j, (half, dst, stationary, moving) in enumerate(todo):
                    last = nc.tensor.matmul(dst, stationary, moving, start=j in first, stop=j in final,
                                            skip_group_check=True)
                last.then_inc(conv_done, 1)

            pe.wait_ge(ident_ready, 1)
            pe.wait_ge(transposed, 3)
            transpose(0, 0, 0)

            def steps(g, last_group):
                for i in range(CG):
                    n = g * CG + i
                    if i + 1 < CG or not last_group:
                        transpose(n + 1, (i + 1) % 3, (i + 1) % 2)
                    if i % CHUNK == 0:
                        pe.wait_ge(band_loaded[i // CHUNK], (g + 1) * (16 * TW))
                    convolve(n, i)

            with pe.Fori(0, GROUPS - 1) as g:
                steps(g, False)
            steps(GROUPS - 1, True)


_INS = ['x', 'L0_conv_w77', 'L0_conv_b77', 'L0_conv_w53', 'L0_conv_b53', 'L0_conv_w35', 'L0_conv_b35',
        'L0_conv_w7w', 'L0_conv_w7h', 'L0_conv_w5w', 'L0_conv_w5h']


def kernel(**inputs):
    import numpy as _np
    import concourse.bacc as _bacc
    from concourse import mybir as _mybir
    from concourse.bass_utils import run_bass_kernel_spmd as _run

    nc = _bacc.Bacc("TRN2", target_bir_lowering=False, num_devices=1)
    arrays, args = {}, []
    for name in _INS:
        a = _np.asarray(inputs[name])
        if a.ndim == 4 and name != 'x':
            a = a[:, :, ::-1, ::-1]
        a = _np.ascontiguousarray(a)
        arrays[f"in_{name}_dram"] = a
        args.append(nc.dram_tensor(f"in_{name}_dram", a.shape, _mybir.dt.from_np(a.dtype), kind="ExternalInput").ap())
    shape = arrays["in_x_dram"].shape
    args.append(nc.dram_tensor("out_0_dram", shape, _mybir.dt.float32, kind="ExternalOutput").ap())
    bass_groupnorm_dwconv_kernel(nc, *args)
    r = _run(nc, [arrays], core_ids=[0])
    return r.results[0]["out_0_dram"]
```

```python
import concourse.bass as bass
from concourse import mybir
from contextlib import ExitStack


def bass_groupnorm_dwconv_kernel(nc: bass.Bass, x, w77, b77, w53, b53, w35, b35, w7w, w7h, w5w, w5h, out):
    fp32 = mybir.dt.float32
    fp16 = mybir.dt.float16
    ALU = mybir.AluOpType
    ACT = mybir.ActivationFunctionType
    AX = mybir.AxisListType

    B, C, H, W = x.shape
    P = 128
    GROUPS = 32
    CG = C // GROUPS
    Q = P // B
    ROWS = H // Q
    PIX = ROWS * W
    TW = 8
    NT = W // TW
    HR = ROWS // 2
    GAP = P - HR * TW
    PAD = 3
    TAPS = 2 * PAD + 1
    OW = TW + 2 * PAD
    OR = ROWS + 2 * PAD
    BAND = OR * OW
    HALF = W // 2
    BANK = 512
    SEG = 4 * TW
    HALO_AT = {(False, 0): (0, 0), (False, 1): (0, SEG), (True, 0): (P - SEG, P - SEG), (True, 1): (P - SEG, P - 2 * SEG)}
    CB = C // P

    CHUNK = 4
    NCH = CG // CHUNK
    LOAD_AT = (8, 9, 10, 11)
    XRING = 4
    STAT = 448
    NSTAT = CG * PIX // STAT
    PER_STEP = 2
    EARLY = 7
    N_EARLY = (CG - EARLY) * PER_STEP
    LATE = (NSTAT - N_EARLY) // PER_STEP
    VAR_AT = LATE + 3
    MATS_AT = {8: (1, 0), 0: (0, 1), 4: (0, 2)}
    EPS = 1e-5
    XSCALE = 256.0
    KSCALE = 16384.0

    taps_strip = nc.dram_tensor("taps_strip", [C * 2 * BAND + BAND], fp16, kind="Internal").ap()
    chan_dram = nc.dram_tensor("chan_dram", [2, C], fp32, kind="Internal").ap()
    stats_dram = nc.dram_tensor("stats_dram", [P, 3], fp32, kind="Internal").ap()

    ctx = ExitStack()
    with ctx:
        def sb(name, shape, dt):
            return ctx.enter_context(nc.sbuf_tensor(name, shape, dt))

        def sem(name):
            return ctx.enter_context(nc.semaphore(name))

        xin = sb("xin", [P, XRING, CG, PIX], fp32)
        xnorm = sb("xnorm", [P, 3, NT * P], fp32)
        xT = sb("xT", [P, 2, 2, NT * P], fp16)
        halo = sb("halo", [P, 2, NT * P], fp16)
        band = sb("band", [P, CG, 2, BAND], fp16)
        edge = sb("edge", [P, CG, 2, 2, PAD * OW], fp16)
        y = sb("y", [P, 2, PIX], fp32)
        chan = sb("chan", [P, 2, C], fp32)
        norm = sb("norm", [P, 2, 2], fp32)
        bns = sb("bns", [P, NSTAT, 6], fp32)
        triple = sb("triple", [P, 3], fp32)
        quad = sb("quad", [P, Q, 3], fp32)
        mv = sb("mv", [P, 2], fp32)
        tmp = sb("tmp", [P, 4], fp32)
        root = sb("root", [P, 1], fp32)
        pace = sb("pace", [P, 1], fp32)
        ident = sb("ident", [P, P], fp32)
        k77 = sb("k77", [P, CB, TAPS, TAPS], fp32)
        k53 = sb("k53", [P, CB, 5, 3], fp32)
        k35 = sb("k35", [P, CB, 3, 5], fp32)
        k7w = sb("k7w", [P, CB, 7], fp32)
        k7h = sb("k7h", [P, CB, 7], fp32)
        k5w = sb("k5w", [P, CB, 5], fp32)
        k5h = sb("k5h", [P, CB, 5], fp32)
        tail = sb("tail", [1, BAND], fp16)
        bia = sb("bia", [P, 3, CB], fp32)
        outer7 = sb("outer7", [P, CB, 7, 7], fp32)
        outer5 = sb("outer5", [P, CB, 5, 5], fp32)
        kabs = sb("kabs", [P, CB, TAPS * TAPS], fp32)
        kmax = sb("kmax", [P, CB], fp32)
        krec = sb("krec", [P, CB], fp32)
        chcol = sb("chcol", [P, 2, CB], fp32)
        strip = sb("strip", [P, CB, 2, BAND], fp16)

        tps = ctx.enter_context(nc.psum_tensor("tps", [P, 2, 2 * BANK], fp32))
        cps = ctx.enter_context(nc.psum_tensor("cps", [P, 2, 2, BANK], fp32))

        weights_loaded = sem("weights_loaded")
        strip_zeroed = sem("strip_zeroed")
        ident_zeroed = sem("ident_zeroed")
        ident_ready = sem("ident_ready")
        setup_step = sem("setup_step")
        strip_ready = sem("strip_ready")
        chcol_ready = sem("chcol_ready")
        strip_saved = sem("strip_saved")
        chan_saved = sem("chan_saved")
        chan_loaded = sem("chan_loaded")
        x_loaded = [sem(f"x_loaded{q}") for q in range(Q)]
        x_stored = [sem(f"x_stored{k}") for k in range(NCH)]
        band_loaded = [sem(f"band_loaded{k}") for k in range(NCH)]
        triple_ready = sem("triple_ready")
        triple_saved = sem("triple_saved")
        quad_loaded = sem("quad_loaded")
        stat_step = sem("stat_step")
        var_ready = sem("var_ready")
        root_ready = sem("root_ready")
        norm_ready = sem("norm_ready")
        xnorm_ready = sem("xnorm_ready")
        transposed = sem("transposed")
        lo_ready = sem("lo_ready")
        conv_done = sem("conv_done")
        y_ready = sem("y_ready")
        sum_done = sem("sum_done")
        hi_ready = sem("hi_ready")
        halo_zeroed = sem("halo_zeroed")
        edge_zeroed = sem("edge_zeroed")
        band_zeroed = sem("band_zeroed")
        xnorm_zeroed = sem("xnorm_zeroed")
        halo_ready = sem("halo_ready")
        edge_ready = sem("edge_ready")

        N_STAT_STEPS = 8

        def x_block(dram, g, q, k, chunk):
            return bass.AP(dram.tensor, (g * CG + k) * H * W + q * PIX,
                           [[C * H * W, B], [H * W, chunk], [1, PIX]])

        def x_slot(g, q, k, chunk):
            return xin[q * B:(q + 1) * B, bass.ds(g % XRING, 1), k:k + chunk, :]

        def halo_copy(slot, part, below):
            src_p, dst_p = HALO_AT[below, part]
            dst = halo[dst_p:dst_p + SEG, slot, :].rearrange("p (t c) -> p t c", c=P)
            src = xT[src_p:src_p + SEG, slot, part, :].rearrange("p (t c) -> p t c", c=P)
            return (dst[:, :, 0:P - B], src[:, :, B:P]) if below else (dst[:, :, B:P], src[:, :, 0:P - B])

        block = ctx.enter_context(nc.Block())

        @block.sync
        def _(sp):
            small = [(k77[:, :, :, :], w77, 49), (k53[:, :, :, :], w53, 15), (k35[:, :, :, :], w35, 15),
                     (k7w[:, :, :], w7w, 7), (k7h[:, :, :], w7h, 7), (k5w[:, :, :], w5w, 5), (k5h[:, :, :], w5h, 5),
                     (bia[:, 0, :], b77, 1), (bia[:, 1, :], b53, 1), (bia[:, 2, :], b35, 1)]
            for dst, src, n in small:
                sp.dma_start(dst, bass.AP(src.tensor, 0, [[CB * n, P], [1, CB * n]])).then_inc(weights_loaded, 16)
            sp.wait_ge(strip_ready, 1)
            sp.wait_ge(strip_zeroed, 1)
            sp.dma_start(bass.AP(taps_strip.tensor, 0, [[CB * 2 * BAND, P], [1, CB * 2 * BAND]]),
                         strip[:, :, :, :]).then_inc(strip_saved, 16)
            sp.dma_start(bass.AP(taps_strip.tensor, C * 2 * BAND, [[BAND, 1], [1, BAND]]),
                         tail[:, :]).then_inc(strip_saved, 16)

            def load_band(g, k):
                n = CHUNK * 2 * BAND
                dst = band[:, k * CHUNK:(k + 1) * CHUNK, :, :].rearrange("p c a n -> p (c a n)")
                base = (g * CG + k * CHUNK) * 2 * BAND
                for p0, h0, rows in ((0, 0, HR), (GAP, HR, HR)):
                    sp.dma_start(dst[p0:p0 + rows * TW, :],
                                 bass.AP(taps_strip.tensor, base + h0 * OW,
                                         [[OW, rows], [1, TW], [1, n]])).then_inc(band_loaded[k], 16)

            def share_triples(g):
                sp.wait_ge(triple_ready, g + 1)
                sp.dma_start(bass.AP(stats_dram.tensor, 0, [[3, Q], [3 * Q, B], [1, 3]]),
                             triple[:, :]).then_inc(triple_saved, 16)

            def fetch_quads(g):
                sp.wait_ge(triple_saved, (g + 1) * 16)
                sp.dma_start(quad[:, :, :].rearrange("p q v -> p (q v)"),
                             bass.AP(stats_dram.tensor, 0, [[0, Q], [3 * Q, B], [1, 3 * Q]])).then_inc(quad_loaded, 16)

            def store(g, k):
                sp.wait_ge(sum_done, g * CG + (k + 1) * CHUNK + 2)
                for q in (0, 2, 1, 3):
                    sp.dma_start(x_block(out, g, q, k * CHUNK, CHUNK), x_slot(g, q, k * CHUNK, CHUNK)).then_inc(x_stored[k], 16)

            sp.wait_ge(strip_saved, 32)
            sp.wait_ge(band_zeroed, 1)
            for k in range(NCH):
                load_band(0, k)
            share_triples(0)
            fetch_quads(0)
            def steps(g, first):
                for k in range(NCH):
                    sp.wait_ge(conv_done, g * CG + (k + 1) * CHUNK + 2)
                    sp.wait_ge(band_loaded[k], (g + 1) * 32)
                    load_band(g + 1, k)
                    if not first:
                        sp.wait_ge(x_stored[k], g * (16 * Q))
                    store(g, k)
                    if k == 0:
                        share_triples(g + 1)
                        fetch_quads(g + 1)

            steps(0, True)
            with sp.Fori(1, GROUPS - 1) as g:
                steps(g, False)
            for k in range(NCH):
                sp.wait_ge(x_stored[k], (GROUPS - 1) * (16 * Q))
                store(GROUPS - 1, k)
            for k in range(NCH):
                sp.wait_ge(x_stored[k], GROUPS * (16 * Q))

        @block.gpsimd
        def _(pool):
            nc.gpsimd.memset(ident[:, :], 0.0).then_inc(ident_zeroed, 1)
            nc.gpsimd.memset(tail[:, :], 0.0)
            nc.gpsimd.memset(strip[:, :, :, :], 0.0).then_inc(strip_zeroed, 1)
            pool.wait_ge(ident_zeroed, 1)
            nc.gpsimd.affine_select(out=ident[:, :], in_=ident[:, :], compare_op=ALU.not_equal, fill=1.0,
                                    base=0, pattern=[[-1, P]], channel_multiplier=1).then_inc(ident_ready, 1)
            nc.gpsimd.memset(band[:, :, :, :], 0.0).then_inc(band_zeroed, 1)
            nc.gpsimd.memset(xnorm[:, :, :], 0.0).then_inc(xnorm_zeroed, 1)
            nc.gpsimd.memset(halo[:, :, :], 0.0).then_inc(halo_zeroed, 1)
            nc.gpsimd.memset(edge[:, :, :, :, :], 0.0).then_inc(edge_zeroed, 1)
            nc.gpsimd.memset(y[:, 1, 0:1], 0.0).then_inc(conv_done, 2)
            pool.wait_ge(halo_zeroed, 1)
            nc.gpsimd.memset(y[:, 0, 0:1], 0.0).then_inc(sum_done, 2)

            def steps(g):
                for i in range(CG):
                    n = g * CG + i
                    pool.wait_ge(y_ready, n + 3)
                    xs = xin[:, bass.ds(g % XRING, 1), i, :].rearrange("p a n -> p (a n)")
                    nc.gpsimd.tensor_tensor(xs, xs, y[:, i % 2, :], ALU.add).then_inc(sum_done, 1)

            with pool.Fori(0, GROUPS) as g:
                steps(g)

        @block.scalar
        def _(act):
            def load(g, q, k, chunk):
                act.dma_start(x_slot(g, q, k, chunk), x_block(x, g, q, k, chunk)).then_inc(x_loaded[q], 16)

            def normalise(g, i, slot):
                xs = xin[:, bass.ds(g % XRING, 1), i, :].rearrange("p a (h t w) -> p (a t) h w", h=ROWS, w=TW)
                nrm = norm[:, bass.ds(g % 2, 1), :].rearrange("p a n -> p (a n)")
                tiles = xnorm[:, slot, ::-1]
                tiles = bass.AP(tiles.tensor, tiles.offset, [tiles.ap[0], [-P, NT], [-GAP, 2], [-1, HR * TW]])
                nc.scalar.activation(tiles, xs, ACT.Identity, bias=nrm[:, 1:2],
                                     scale=nrm[:, 0:1]).then_inc(xnorm_ready, 1)

            def high(slot):
                nc.scalar.activation(xT[:, slot, 0, :], tps[:, slot, 0:NT * P], ACT.Copy).then_inc(hi_ready, 1)

            for k in range(0, CG, CHUNK):
                for q in (0, 2, 1, 3):
                    if k:
                        act.wait_ge(x_loaded[q], 16 * (k // CHUNK))
                    load(0, q, k, CHUNK)
            for q in (0, 2, 1, 3):
                act.wait_ge(x_loaded[q], 16 * NCH)
                load(1, q, 0, CG)
            act.wait_ge(chcol_ready, 1)
            act.dma_start(bass.AP(chan_dram.tensor, 0, [[CB, P], [C, 2], [1, CB]]), chcol[:, :, :]).then_inc(chan_saved, 16)

            def standard_deviation(g):
                act.wait_ge(var_ready, g + 1)
                nc.scalar.activation(root[:, :], tmp[:, 0:1], ACT.Sqrt).then_inc(root_ready, 1)

            act.wait_ge(chan_saved, 16)
            act.dma_start(chan[:, :, :], bass.AP(chan_dram.tensor, 0, [[0, P], [1, 2 * C]])).then_inc(chan_loaded, 16)
            standard_deviation(0)
            act.wait_ge(norm_ready, 1)
            act.wait_ge(xnorm_zeroed, 1)
            act.wait_ge(transposed, 3)
            normalise(0, 0, 0)
            normalise(0, 1, 1)
            act.wait_ge(transposed, 4)
            act.wait_ge(conv_done, 2)
            high(0)
            act.wait_ge(chan_loaded, 16)

            def load_ahead(g, q):
                act.wait_ge(x_loaded[q], (g - 1 + NCH) * 16)
                load(g, q, 0, CG)

            def steps(g, last):
                for i in range(CG):
                    n = g * CG + i
                    if type(g) is int and g == 0:
                        if i < Q:
                            load_ahead(2, i)
                        elif i >= CG - Q:
                            load_ahead(3, i - (CG - Q))
                    elif i in LOAD_AT and not (type(g) is int and g + 3 >= GROUPS):
                        if i == LOAD_AT[0]:
                            for k in range(NCH):
                                act.wait_ge(x_stored[k], g * (16 * Q))
                        load_ahead(g + 3, LOAD_AT.index(i))
                    if i + 1 < CG or not last:
                        act.wait_ge(transposed, n + 5)
                        act.wait_ge(conv_done, n + 2)
                        high((i + 1) % 2)
                    if i + 2 < CG or not last:
                        act.wait_ge(transposed, n + 3)
                        if i + 2 < CG:
                            normalise(g, i + 2, (i + 2) % 3)
                        else:
                            act.wait_ge(norm_ready, g + 2)
                            normalise(g + 1, i + 2 - CG, (i + 2) % 3)
                    act.wait_ge(conv_done, n + 3)
                    act.wait_ge(sum_done, n + 1)
                    nc.scalar.activation(y[:, i % 2, :].rearrange("p (h a w) -> p a h w", h=ROWS, w=HALF),
                                         cps[:, i % 2, :, 0:ROWS * HALF].rearrange("p a (h w) -> p a h w", w=HALF),
                                         ACT.Identity, bias=chan[:, 1, bass.ds(n, 1)],
                                         scale=chan[:, 0, bass.ds(n, 1)]).then_inc(y_ready, 1)
                    if not last and i == VAR_AT:
                        standard_deviation(g + 1)

            steps(0, False)
            with act.Fori(1, GROUPS - 3) as g:
                steps(g, False)
            for g in range(GROUPS - 3, GROUPS):
                steps(g, g == GROUPS - 1)

        @block.vector
        def _(dve):
            done = [0]

            def link(ins):
                done[0] += 1
                ins.then_inc(setup_step, 1)
                dve.wait_ge(setup_step, done[0])

            nc.vector.memset(tmp[:, 0:1], 0.0).then_inc(lo_ready, 2)
            nc.vector.memset(tmp[:, 1:2], 0.0).then_inc(y_ready, 2)
            nc.vector.memset(tmp[:, 2:3], 0.0).then_inc(transposed, 3)
            link(nc.vector.memset(triple[:, 0:1], 1.0))

            dve.wait_ge(weights_loaded, 160)
            nc.vector.tensor_tensor(outer7[:, :, :, :], k7h[:, :, :].unsqueeze(3).to_broadcast([P, CB, 7, 7]),
                                    k7w[:, :, :].unsqueeze(2).to_broadcast([P, CB, 7, 7]), ALU.mult)
            link(nc.vector.tensor_tensor(outer5[:, :, :, :], k5h[:, :, :].unsqueeze(3).to_broadcast([P, CB, 5, 5]),
                                         k5w[:, :, :].unsqueeze(2).to_broadcast([P, CB, 5, 5]), ALU.mult))
            link(nc.vector.tensor_tensor(k77[:, :, 1:6, 2:5], k77[:, :, 1:6, 2:5], k53[:, :, :, :], ALU.add))
            link(nc.vector.tensor_tensor(k77[:, :, 2:5, 1:6], k77[:, :, 2:5, 1:6], k35[:, :, :, :], ALU.add))
            link(nc.vector.tensor_tensor(k77[:, :, :, :], k77[:, :, :, :], outer7[:, :, :, :], ALU.add))
            link(nc.vector.tensor_tensor(k77[:, :, 1:6, 1:6], k77[:, :, 1:6, 1:6], outer5[:, :, :, :], ALU.add))
            flat = k77[:, :, :, :].rearrange("p c a b -> p c (a b)")
            link(nc.vector.scalar_tensor_tensor(out=kabs[:, :, :], in0=flat, scalar=-1.0, in1=flat, op0=ALU.mult, op1=ALU.max))
            link(nc.vector.tensor_reduce(kmax[:, :], kabs[:, :, :], AX.X, ALU.max))
            link(nc.vector.tensor_scalar(kmax[:, :], kmax[:, :], 1e-30, None, ALU.max))
            link(nc.vector.reciprocal(krec[:, :], kmax[:, :]))
            link(nc.vector.tensor_scalar(krec[:, :], krec[:, :], KSCALE, None, ALU.mult))
            link(nc.vector.tensor_tensor(kabs[:, :, :], flat, krec[:, :].unsqueeze(2).to_broadcast([P, CB, 49]), ALU.mult))
            dve.wait_ge(strip_zeroed, 1)
            hi, lo = [strip[:, :, part, :].rearrange("p c (a b) -> p c a b", b=OW)[:, :, OR - TAPS:, OW - TAPS:]
                      for part in range(2)]
            scaled = kabs[:, :, :].rearrange("p c (a b) -> p c a b", b=TAPS)
            link(nc.vector.tensor_copy(hi, scaled))
            nc.vector.tensor_tensor(lo, scaled, hi, ALU.subtract).then_inc(strip_ready, 1)
            nc.vector.tensor_scalar(chcol[:, 0, :], kmax[:, :], 1.0 / (KSCALE * XSCALE), None, ALU.mult)
            link(nc.vector.tensor_tensor(bia[:, 0, :], bia[:, 0, :], bia[:, 1, :], ALU.add))
            nc.vector.tensor_tensor(chcol[:, 1, :], bia[:, 0, :], bia[:, 2, :], ALU.add).then_inc(chcol_ready, 1)

            def statistics(g, s):
                if type(g) is int and g == 0:
                    if s * STAT % (CHUNK * PIX) == 0:
                        for q in range(Q):
                            dve.wait_ge(x_loaded[q], 16 * (s * STAT // (CHUNK * PIX) + 1))
                elif s == 0:
                    for q in range(Q):
                        dve.wait_ge(x_loaded[q], (g + NCH) * 16)
                xg = xin[:, bass.ds(g % XRING, 1), :, :].rearrange("p a c n -> p (a c n)")
                return nc.vector.bn_stats(bns[:, s, :], xg[:, s * STAT:(s + 1) * STAT])

            def aggregate(g):
                dve.wait_ge(stat_step, N_STAT_STEPS * g + 1)
                nc.vector.memset(pace[:, :], 0.0)
                nc.vector.bn_aggr(triple[:, 1:3], bns[:, :, :].rearrange("p s v -> p (s v)")).then_inc(triple_ready, 1)

            ve, r0, u = tmp[:, 0:1], tmp[:, 1:2], tmp[:, 2:3]

            def variance(g):
                dve.wait_ge(quad_loaded, (g + 1) * 16)
                nc.vector.memset(pace[:, :], 0.0)
                nc.vector.bn_aggr(mv[:, :], quad[:, :, :].rearrange("p q v -> p (q v)")).then_inc(stat_step, 1)
                dve.wait_ge(stat_step, N_STAT_STEPS * g + 2)
                nc.vector.tensor_scalar(ve, mv[:, 1:2], EPS, None, ALU.add).then_inc(var_ready, 1)

            def finish_norm(g):
                step = N_STAT_STEPS * g + 2
                nrm = norm[:, bass.ds(g % 2, 1), :].rearrange("p a n -> p (a n)")
                dve.wait_ge(root_ready, g + 1)
                nc.vector.reciprocal(r0, root[:, :]).then_inc(stat_step, 1)
                dve.wait_ge(stat_step, step + 1)
                nc.vector.tensor_tensor(u, r0, r0, ALU.mult).then_inc(stat_step, 1)
                dve.wait_ge(stat_step, step + 2)
                nc.vector.tensor_tensor(u, u, ve, ALU.mult).then_inc(stat_step, 1)
                dve.wait_ge(stat_step, step + 3)
                nc.vector.tensor_scalar(u, u, -0.5 * XSCALE, 1.5 * XSCALE, ALU.mult, ALU.add).then_inc(stat_step, 1)
                dve.wait_ge(stat_step, step + 4)
                nc.vector.tensor_tensor(nrm[:, 0:1], r0, u, ALU.mult).then_inc(stat_step, 1)
                dve.wait_ge(stat_step, step + 5)
                nc.vector.tensor_tensor(u, mv[:, 0:1], nrm[:, 0:1], ALU.mult).then_inc(stat_step, 1)
                dve.wait_ge(stat_step, step + 6)
                nc.vector.tensor_scalar(nrm[:, 1:2], u, -1.0, None, ALU.mult).then_inc(norm_ready, 1)

            def low(n, slot):
                dve.wait_ge(hi_ready, n + 1)
                nc.vector.tensor_tensor(xT[:, slot, 1, :], tps[:, slot, 0:NT * P], xT[:, slot, 0, :],
                                        ALU.subtract).then_inc(lo_ready, 1)

            def halo_parts(n, slot):
                for below in (False, True):
                    dst, src = halo_copy(slot, 0, below)
                    nc.vector.tensor_copy(dst, src)
                dve.wait_ge(lo_ready, n + 3)
                for below in (False, True):
                    dst, src = halo_copy(slot, 1, below)
                    ins = nc.vector.tensor_copy(dst, src)
                ins.then_inc(halo_ready, 1)

            def edge_matrices(g, k):
                dve.wait_ge(band_loaded[k], (g + 1) * 32)
                if not (type(g) is int and g == 0):
                    dve.wait_ge(conv_done, (g - 1) * CG + (k + 1) * CHUNK + 2)
                ch = slice(k * CHUNK, (k + 1) * CHUNK)
                top = (PAD + ROWS) * OW
                for below, m0 in ((False, top), (True, 0)):
                    src_p, lo_p = HALO_AT[below, 1]
                    m = band[src_p:src_p + SEG, ch, :, m0:m0 + PAD * OW]
                    nc.vector.tensor_copy(edge[src_p:src_p + SEG, ch, :, int(below), :], m)
                    ins = nc.vector.tensor_copy(edge[lo_p:lo_p + SEG, ch, 0, int(below), :], m[:, :, 0, :])
                ins.then_inc(edge_ready, 1)

            for s in range(NSTAT):
                last = statistics(0, s)
            last.then_inc(stat_step, 1)
            aggregate(0)
            variance(0)
            finish_norm(0)
            dve.wait_ge(edge_zeroed, 1)
            edge_matrices(0, 0)
            low(0, 0)
            dve.wait_ge(halo_zeroed, 1)
            halo_parts(0, 0)

            def steps(g):
                first = type(g) is int and g == 0
                more = [not (type(g) is int and g + ahead >= GROUPS) for ahead in range(3)]
                for i in range(CG):
                    if i == VAR_AT + 1 and more[1]:
                        finish_norm(g + 1)
                    if i + 1 < CG or more[1]:
                        low(g * CG + i + 1, (i + 1) % 2)
                        halo_parts(g * CG + i + 1, (i + 1) % 2)
                    if i in MATS_AT and more[MATS_AT[i][0]]:
                        edge_matrices(g + MATS_AT[i][0], MATS_AT[i][1])
                    if i == VAR_AT and more[1]:
                        variance(g + 1)
                    if i <= LATE and more[1]:
                        n = NSTAT // LATE if first else PER_STEP
                        start = i * n + (0 if first else N_EARLY)
                        for s in range(start, min(start + n, NSTAT)):
                            last = statistics(g + 1, s)
                        if i == LATE:
                            last.then_inc(stat_step, 1)
                            dve.wait_ge(triple_saved, (g + 1) * 16)
                            aggregate(g + 1)
                    if i >= EARLY and more[2]:
                        if i == EARLY:
                            dve.wait_ge(triple_ready, g + 2)
                        for s in range((i - EARLY) * PER_STEP, (i - EARLY + 1) * PER_STEP):
                            statistics(g + 2, s)

            steps(0)
            with dve.Fori(1, GROUPS - 2) as g:
                steps(g)
            steps(GROUPS - 2)
            steps(GROUPS - 1)

        @block.tensor
        def _(pe):
            def transpose(n, xslot, slot):
                pe.wait_ge(xnorm_ready, n + 1)
                pe.wait_ge(lo_ready, n + 1)
                for t in range(NT):
                    last = nc.tensor.transpose(tps[:, slot, t * P:(t + 1) * P],
                                               xnorm[:, xslot, t * P:(t + 1) * P], ident[:, :])
                last.then_inc(transposed, 1)

            spans = []
            for t in range(NT):
                reach = W - (t + 1) * TW - PAD
                for half in range(2):
                    lo, hi = max(reach, half * HALF), min(reach + OW, (half + 1) * HALF)
                    if lo < hi:
                        spans.append((t, half, lo - half * HALF, hi - lo, lo - reach))

            def convolve(n, i):
                slot = i % 2
                pe.wait_ge(hi_ready, n + 1)
                pe.wait_ge(y_ready, n + 1)
                started = set()
                for xpart, kpart in ((0, 0), (0, 1), (1, 0)):
                    if xpart == 1:
                        pe.wait_ge(lo_ready, n + 3)
                    mat = band[:, i, kpart, :].rearrange("p (h w) -> p h w", w=OW)[:, PAD:PAD + ROWS, :]
                    for t, half, col, cols, off in spans:
                        dst = cps[:, slot, half, 0:ROWS * HALF].rearrange("p (h w) -> p h w", w=HALF)
                        nc.tensor.matmul(dst[:, :, col:col + cols], xT[:, slot, xpart, t * P:(t + 1) * P],
                                         mat[:, :, off:off + cols], start=half not in started, stop=False,
                                         skip_group_check=True)
                        started.add(half)
                pe.wait_ge(halo_ready, n + 1)
                for kpart in range(2):
                    mat = edge[:, i, kpart, :, :].rearrange("p e (h w) -> p e h w", w=OW)
                    for j, (t, half, col, cols, off) in enumerate(spans):
                        dst = cps[:, slot, half, col:col + cols]
                        dst = bass.AP(dst.tensor, dst.offset,
                                      [dst.ap[0], [(ROWS - PAD) * HALF, 2], [HALF, PAD], [1, cols]])
                        stop = kpart == 1 and not any(s[1] == half for s in spans[j + 1:])
                        last = nc.tensor.matmul(dst, halo[:, slot, t * P:(t + 1) * P], mat[:, :, :, off:off + cols],
                                                start=False, stop=stop, skip_group_check=True)
                last.then_inc(conv_done, 1)

            pe.wait_ge(ident_ready, 1)
            pe.wait_ge(transposed, 3)
            transpose(0, 0, 0)

            def steps(g, last_group):
                for i in range(CG):
                    n = g * CG + i
                    if i + 1 < CG or not last_group:
                        transpose(n + 1, (i + 1) % 3, (i + 1) % 2)
                    if i % CHUNK == 0:
                        pe.wait_ge(band_loaded[i // CHUNK], (g + 1) * 32)
                        pe.wait_ge(edge_ready, g * NCH + i // CHUNK + 1)
                    convolve(n, i)

            with pe.Fori(0, GROUPS - 1) as g:
                steps(g, False)
            steps(GROUPS - 1, True)


_INS = ['x', 'L0_conv_w77', 'L0_conv_b77', 'L0_conv_w53', 'L0_conv_b53', 'L0_conv_w35', 'L0_conv_b35',
        'L0_conv_w7w', 'L0_conv_w7h', 'L0_conv_w5w', 'L0_conv_w5h']


def kernel(**inputs):
    import numpy as _np
    import concourse.bacc as _bacc
    from concourse import mybir as _mybir
    from concourse.bass_utils import run_bass_kernel_spmd as _run

    nc = _bacc.Bacc("TRN2", target_bir_lowering=False, num_devices=1)
    arrays, args = {}, []
    for name in _INS:
        a = _np.asarray(inputs[name])
        if a.ndim == 4 and name != 'x':
            a = a[:, :, ::-1, ::-1]
        a = _np.ascontiguousarray(a)
        arrays[f"in_{name}_dram"] = a
        args.append(nc.dram_tensor(f"in_{name}_dram", a.shape, _mybir.dt.from_np(a.dtype), kind="ExternalInput").ap())
    shape = arrays["in_x_dram"].shape
    args.append(nc.dram_tensor("out_0_dram", shape, _mybir.dt.float32, kind="ExternalOutput").ap())
    bass_groupnorm_dwconv_kernel(nc, *args)
    r = _run(nc, [arrays], core_ids=[0])
    return r.results[0]["out_0_dram"]
```

```python
import concourse.bass as bass
from concourse import mybir
from contextlib import ExitStack


def bass_groupnorm_dwconv_kernel(nc: bass.Bass, x, w77, b77, w53, b53, w35, b35, w7w, w7h, w5w, w5h, out):
    fp32 = mybir.dt.float32
    fp16 = mybir.dt.float16
    ALU = mybir.AluOpType
    ACT = mybir.ActivationFunctionType
    AX = mybir.AxisListType

    B, C, H, W = x.shape
    P = 128
    GROUPS = 32
    CG = C // GROUPS
    Q = P // B
    ROWS = H // Q
    PIX = ROWS * W
    TW = 8
    NT = W // TW
    HR = ROWS // 2
    GAP = P - HR * TW
    PAD = 3
    TAPS = 2 * PAD + 1
    OW = TW + 2 * PAD
    OR = ROWS + 2 * PAD
    BAND = OR * OW
    HALF = W // 2
    BANK = 512
    SEG = 4 * TW
    HALO_AT = {(False, 0): (0, 0), (False, 1): (0, SEG), (True, 0): (P - SEG, P - SEG), (True, 1): (P - SEG, P - 2 * SEG)}
    CB = C // P

    CHUNK = 4
    NCH = CG // CHUNK
    LOAD_AT = (8, 9, 10, 11)
    XRING = 4
    STAT = 448
    NSTAT = CG * PIX // STAT
    PIECES = (2, 2, 2, 2, 1, 2, 2, 2, 1, 2, 1, 2)
    EARLY = 5
    LATE = EARLY - 1
    N_EARLY = sum(PIECES[EARLY:])
    assert len(PIECES) == CG and sum(PIECES) == NSTAT
    VAR_AT = LATE + 3
    MATS_AT = {10: (1, 0), 1: (0, 1), 4: (0, 2)}
    FIRST = CHUNK * PIX // STAT
    FIRST_EARLY = 7
    FIRST_PER_STEP = 3
    POOL_COPIES = (1, 2, 4, 5, 7, 8, 9, 10, 11)
    EPS = 1e-5
    XSCALE = 256.0
    KSCALE = 16384.0

    taps_strip = nc.dram_tensor("taps_strip", [C * 2 * BAND + BAND], fp16, kind="Internal").ap()
    chan_dram = nc.dram_tensor("chan_dram", [2, C], fp32, kind="Internal").ap()
    stats_dram = nc.dram_tensor("stats_dram", [P, 3], fp32, kind="Internal").ap()

    ctx = ExitStack()
    with ctx:
        def sb(name, shape, dt):
            return ctx.enter_context(nc.sbuf_tensor(name, shape, dt))

        def sem(name):
            return ctx.enter_context(nc.semaphore(name))

        xin = sb("xin", [P, XRING, CG, PIX], fp32)
        xnorm = sb("xnorm", [P, 3, NT * P], fp32)
        xT = sb("xT", [P, 2, 2, NT * P], fp16)
        halo = sb("halo", [P, 2, NT * P], fp16)
        band = sb("band", [P, CG, 2, BAND], fp16)
        edge = sb("edge", [P, CG, 2, 2, PAD * OW], fp16)
        y = sb("y", [P, 2, PIX], fp32)
        chan = sb("chan", [P, 2, C], fp32)
        norm = sb("norm", [P, 2, 2], fp32)
        bns = sb("bns", [P, NSTAT, 6], fp32)
        triple = sb("triple", [P, 3], fp32)
        quad = sb("quad", [P, Q, 3], fp32)
        mv = sb("mv", [P, 2], fp32)
        tmp = sb("tmp", [P, 4], fp32)
        root = sb("root", [P, 1], fp32)
        warm = sb("warm", [P, 2], fp32)
        pace = sb("pace", [P, 1], fp32)
        ones = sb("ones", [P, NT], fp16)
        ident = sb("ident", [P, P], fp32)
        k77 = sb("k77", [P, CB, TAPS, TAPS], fp32)
        k53 = sb("k53", [P, CB, 5, 3], fp32)
        k35 = sb("k35", [P, CB, 3, 5], fp32)
        k7w = sb("k7w", [P, CB, 7], fp32)
        k7h = sb("k7h", [P, CB, 7], fp32)
        k5w = sb("k5w", [P, CB, 5], fp32)
        k5h = sb("k5h", [P, CB, 5], fp32)
        tail = sb("tail", [1, BAND], fp16)
        bia = sb("bia", [P, 3, CB], fp32)
        outer7 = sb("outer7", [P, CB, 7, 7], fp32)
        outer5 = sb("outer5", [P, CB, 5, 5], fp32)
        kabs = sb("kabs", [P, CB, TAPS * TAPS], fp32)
        kmax = sb("kmax", [P, CB], fp32)
        krec = sb("krec", [P, CB], fp32)
        chcol = sb("chcol", [P, 2, CB], fp32)
        strip = sb("strip", [P, CB, 2, BAND], fp16)

        tps = ctx.enter_context(nc.psum_tensor("tps", [P, 2, 2 * BANK], fp32))
        cps = ctx.enter_context(nc.psum_tensor("cps", [P, 2, 2, BANK], fp32))

        weights_loaded = sem("weights_loaded")
        strip_zeroed = sem("strip_zeroed")
        ident_zeroed = sem("ident_zeroed")
        ident_ready = sem("ident_ready")
        setup_step = sem("setup_step")
        strip_ready = sem("strip_ready")
        chcol_ready = sem("chcol_ready")
        strip_saved = sem("strip_saved")
        chan_saved = sem("chan_saved")
        chan_loaded = sem("chan_loaded")
        x_loaded = [sem(f"x_loaded{q}") for q in range(Q)]
        x_stored = [sem(f"x_stored{k}") for k in range(NCH)]
        band_loaded = [sem(f"band_loaded{k}") for k in range(NCH)]
        triple_ready = sem("triple_ready")
        triple_saved = sem("triple_saved")
        quad_loaded = sem("quad_loaded")
        stat_step = sem("stat_step")
        var_ready = sem("var_ready")
        warm_set = sem("warm_set")
        root_ready = sem("root_ready")
        norm_ready = sem("norm_ready")
        xnorm_ready = sem("xnorm_ready")
        transposed = sem("transposed")
        lo_ready = sem("lo_ready")
        conv_done = sem("conv_done")
        y_ready = sem("y_ready")
        sum_done = sem("sum_done")
        hi_ready = sem("hi_ready")
        halo_zeroed = sem("halo_zeroed")
        edge_zeroed = sem("edge_zeroed")
        band_zeroed = sem("band_zeroed")
        xnorm_zeroed = sem("xnorm_zeroed")
        halo_above = sem("halo_above")
        halo_rest = sem("halo_rest")
        ones_ready = sem("ones_ready")
        edge_ready = sem("edge_ready")

        N_STAT_STEPS = 6

        def x_block(dram, g, q, k, chunk):
            return bass.AP(dram.tensor, (g * CG + k) * H * W + q * PIX,
                           [[C * H * W, B], [H * W, chunk], [1, PIX]])

        def x_slot(g, q, k, chunk):
            return xin[q * B:(q + 1) * B, bass.ds(g % XRING, 1), k:k + chunk, :]

        def halo_copy(slot, part, below):
            src_p, dst_p = HALO_AT[below, part]
            dst = halo[dst_p:dst_p + SEG, slot, :].rearrange("p (t c) -> p t c", c=P)
            src = xT[src_p:src_p + SEG, slot, part, :].rearrange("p (t c) -> p t c", c=P)
            return (dst[:, :, 0:P - B], src[:, :, B:P]) if below else (dst[:, :, B:P], src[:, :, 0:P - B])

        block = ctx.enter_context(nc.Block())

        @block.sync
        def _(sp):
            small = [(k77[:, :, :, :], w77, 49), (k53[:, :, :, :], w53, 15), (k35[:, :, :, :], w35, 15),
                     (k7w[:, :, :], w7w, 7), (k7h[:, :, :], w7h, 7), (k5w[:, :, :], w5w, 5), (k5h[:, :, :], w5h, 5),
                     (bia[:, 0, :], b77, 1), (bia[:, 1, :], b53, 1), (bia[:, 2, :], b35, 1)]
            for dst, src, n in small:
                sp.dma_start(dst, bass.AP(src.tensor, 0, [[CB * n, P], [1, CB * n]])).then_inc(weights_loaded, 16)

            def load_band(g, k):
                n = CHUNK * 2 * BAND
                dst = band[:, k * CHUNK:(k + 1) * CHUNK, :, :].rearrange("p c a n -> p (c a n)")
                base = (g * CG + k * CHUNK) * 2 * BAND
                for p0, h0, rows in ((0, 0, HR), (GAP, HR, HR)):
                    sp.dma_start(dst[p0:p0 + rows * TW, :],
                                 bass.AP(taps_strip.tensor, base + h0 * OW,
                                         [[OW, rows], [1, TW], [1, n]])).then_inc(band_loaded[k], 16)

            def share_triples(g):
                sp.wait_ge(triple_ready, g + 1)
                sp.dma_start(bass.AP(stats_dram.tensor, 0, [[3, Q], [3 * Q, B], [1, 3]]),
                             triple[:, :]).then_inc(triple_saved, 16)

            def fetch_quads(g):
                sp.wait_ge(triple_saved, (g + 1) * 16)
                sp.dma_start(quad[:, :, :].rearrange("p q v -> p (q v)"),
                             bass.AP(stats_dram.tensor, 0, [[0, Q], [3 * Q, B], [1, 3 * Q]])).then_inc(quad_loaded, 16)

            def store(g, k):
                sp.wait_ge(sum_done, g * CG + (k + 1) * CHUNK + 2)
                for q in (0, 2, 1, 3):
                    sp.dma_start(x_block(out, g, q, k * CHUNK, CHUNK), x_slot(g, q, k * CHUNK, CHUNK)).then_inc(x_stored[k], 16)

            share_triples(0)
            sp.wait_ge(strip_ready, 1)
            sp.wait_ge(strip_zeroed, 1)
            sp.dma_start(bass.AP(taps_strip.tensor, 0, [[CB * 2 * BAND, P], [1, CB * 2 * BAND]]),
                         strip[:, :, :, :]).then_inc(strip_saved, 16)
            sp.dma_start(bass.AP(taps_strip.tensor, C * 2 * BAND, [[BAND, 1], [1, BAND]]),
                         tail[:, :]).then_inc(strip_saved, 16)
            sp.wait_ge(chcol_ready, 1)
            sp.dma_start(bass.AP(chan_dram.tensor, 0, [[CB, P], [C, 2], [1, CB]]), chcol[:, :, :]).then_inc(chan_saved, 16)
            fetch_quads(0)
            sp.wait_ge(strip_saved, 32)
            sp.wait_ge(band_zeroed, 1)
            load_band(0, 0)
            sp.wait_ge(chan_saved, 16)
            sp.dma_start(chan[:, :, :], bass.AP(chan_dram.tensor, 0, [[0, P], [1, 2 * C]])).then_inc(chan_loaded, 16)
            load_band(0, 1)
            for q in range(Q):
                sp.wait_ge(x_loaded[q], (NCH + 1) * 16)
                sp.dma_start(x_slot(1, q, CHUNK, CG - CHUNK), x_block(x, 1, q, CHUNK, CG - CHUNK)).then_inc(x_loaded[q], 16)
            load_band(0, 2)
            for q in range(Q):
                sp.wait_ge(x_loaded[q], (NCH + 2) * 16)
                sp.dma_start(x_slot(2, q, 0, CG), x_block(x, 2, q, 0, CG)).then_inc(x_loaded[q], 16)

            def steps(g, first):
                share_triples(g + 1)
                for k in range(NCH):
                    sp.wait_ge(conv_done, g * CG + (k + 1) * CHUNK + 2)
                    sp.wait_ge(band_loaded[k], (g + 1) * 32)
                    load_band(g + 1, k)
                    if k == 0:
                        fetch_quads(g + 1)
                    if not first:
                        sp.wait_ge(x_stored[k], g * (16 * Q))
                    store(g, k)

            steps(0, True)
            with sp.Fori(1, GROUPS - 1) as g:
                steps(g, False)
            for k in range(NCH - 1):
                sp.wait_ge(x_stored[k], (GROUPS - 1) * (16 * Q))
                store(GROUPS - 1, k)
            half = CHUNK // 2
            for c in (CG - CHUNK, CG - half):
                sp.wait_ge(sum_done, (GROUPS - 1) * CG + c + half + 2)
                for q in (0, 2, 1, 3):
                    sp.dma_start(x_block(out, GROUPS - 1, q, c, half), x_slot(GROUPS - 1, q, c, half)).then_inc(x_stored[NCH - 1], 16)
            for k in range(NCH - 1):
                sp.wait_ge(x_stored[k], GROUPS * (16 * Q))
            sp.wait_ge(x_stored[NCH - 1], (GROUPS + 1) * (16 * Q))

        @block.gpsimd
        def _(pool):
            nc.gpsimd.memset(ident[:, :], 0.0).then_inc(ident_zeroed, 1)
            nc.gpsimd.memset(tail[:, :], 0.0)
            nc.gpsimd.memset(strip[:, :, :, :], 0.0).then_inc(strip_zeroed, 1)
            pool.wait_ge(ident_zeroed, 1)
            nc.gpsimd.affine_select(out=ident[:, :], in_=ident[:, :], compare_op=ALU.not_equal, fill=1.0,
                                    base=0, pattern=[[-1, P]], channel_multiplier=1).then_inc(ident_ready, 1)
            nc.gpsimd.memset(band[:, :, :, :], 0.0).then_inc(band_zeroed, 1)
            nc.gpsimd.memset(xnorm[:, :, :], 0.0).then_inc(xnorm_zeroed, 1)
            nc.gpsimd.memset(ones[:, :], 1.0).then_inc(ones_ready, 1)
            nc.gpsimd.memset(halo[:, :, :], 0.0).then_inc(halo_zeroed, 1)
            nc.gpsimd.memset(edge[:, :, :, :, :], 0.0).then_inc(edge_zeroed, 1)
            nc.gpsimd.memset(y[:, 1, 0:1], 0.0).then_inc(conv_done, 2)
            pool.wait_ge(halo_zeroed, 1)
            pool.wait_ge(ones_ready, 1)
            nc.gpsimd.memset(y[:, 0, 0:1], 0.0).then_inc(sum_done, 2)

            def from_above(n, slot):
                pool.wait_ge(hi_ready, n + 1)
                dst, src = halo_copy(slot, 0, False)
                one = ones[0:SEG, :].unsqueeze(2).to_broadcast([SEG, NT, P - B])
                nc.gpsimd.tensor_tensor(dst, src, one, ALU.mult).then_inc(halo_above, 1)

            def steps(g):
                for i in range(CG):
                    n = g * CG + i
                    if i + 1 in POOL_COPIES:
                        from_above(n + 1, (i + 1) % 2)
                    pool.wait_ge(y_ready, n + 3)
                    xs = xin[:, bass.ds(g % XRING, 1), i, :].rearrange("p a n -> p (a n)")
                    nc.gpsimd.tensor_tensor(xs, xs, y[:, i % 2, :], ALU.add).then_inc(sum_done, 1)

            with pool.Fori(0, GROUPS) as g:
                steps(g)

        @block.scalar
        def _(act):
            def load(g, q, k, chunk):
                act.dma_start(x_slot(g, q, k, chunk), x_block(x, g, q, k, chunk)).then_inc(x_loaded[q], 16)

            def normalise(g, i, slot):
                xs = xin[:, bass.ds(g % XRING, 1), i, :].rearrange("p a (h t w) -> p (a t) h w", h=ROWS, w=TW)
                nrm = norm[:, bass.ds(g % 2, 1), :].rearrange("p a n -> p (a n)")
                tiles = xnorm[:, slot, ::-1]
                tiles = bass.AP(tiles.tensor, tiles.offset, [tiles.ap[0], [-P, NT], [-GAP, 2], [-1, HR * TW]])
                nc.scalar.activation(tiles, xs, ACT.Identity, bias=nrm[:, 1:2],
                                     scale=nrm[:, 0:1]).then_inc(xnorm_ready, 1)

            def high(slot):
                nc.scalar.activation(xT[:, slot, 0, :], tps[:, slot, 0:NT * P], ACT.Copy).then_inc(hi_ready, 1)

            act.wait_ge(warm_set, 1)
            nc.scalar.activation(warm[:, 1:2], warm[:, 0:1], ACT.Sqrt)
            for k in range(0, CG, CHUNK):
                for q in (0, 2, 1, 3):
                    if k:
                        act.wait_ge(x_loaded[q], 16 * (k // CHUNK))
                    load(0, q, k, CHUNK)
            for q in (0, 2, 1, 3):
                act.wait_ge(x_loaded[q], 16 * NCH)
                load(1, q, 0, CHUNK)

            def standard_deviation(g):
                act.wait_ge(var_ready, g + 1)
                nc.scalar.activation(root[:, :], tmp[:, 0:1], ACT.Sqrt).then_inc(root_ready, 1)

            standard_deviation(0)
            act.wait_ge(norm_ready, 1)
            act.wait_ge(xnorm_zeroed, 1)
            act.wait_ge(transposed, 3)
            normalise(0, 0, 0)
            normalise(0, 1, 1)
            act.wait_ge(transposed, 4)
            act.wait_ge(conv_done, 2)
            high(0)
            act.wait_ge(chan_loaded, 16)

            def load_ahead(g, q):
                act.wait_ge(x_loaded[q], (g + NCH) * 16)
                load(g, q, 0, CG)

            def steps(g, last):
                for i in range(CG):
                    n = g * CG + i
                    if i + 2 < CG or not last:
                        act.wait_ge(transposed, n + 3)
                        if i + 2 < CG:
                            normalise(g, i + 2, (i + 2) % 3)
                        else:
                            act.wait_ge(norm_ready, g + 2)
                            normalise(g + 1, i + 2 - CG, (i + 2) % 3)
                    if i + 1 < CG or not last:
                        act.wait_ge(transposed, n + 5)
                        act.wait_ge(conv_done, n + 2)
                        high((i + 1) % 2)
                    if not last and i == VAR_AT + 1:
                        standard_deviation(g + 1)
                    if i in LOAD_AT and not (type(g) is int and g + 3 >= GROUPS):
                        if i == LOAD_AT[0] and not (type(g) is int and g == 0):
                            for k in range(NCH):
                                act.wait_ge(x_stored[k], g * (16 * Q))
                        load_ahead(g + 3, LOAD_AT.index(i))
                    act.wait_ge(conv_done, n + 3)
                    act.wait_ge(sum_done, n + 1)
                    nc.scalar.activation(y[:, i % 2, :].rearrange("p (h a w) -> p a h w", h=ROWS, w=HALF),
                                         cps[:, i % 2, :, 0:ROWS * HALF].rearrange("p a (h w) -> p a h w", w=HALF),
                                         ACT.Identity, bias=chan[:, 1, bass.ds(n, 1)],
                                         scale=chan[:, 0, bass.ds(n, 1)]).then_inc(y_ready, 1)

            steps(0, False)
            with act.Fori(1, GROUPS - 3) as g:
                steps(g, False)
            for g in range(GROUPS - 3, GROUPS):
                steps(g, g == GROUPS - 1)

        @block.vector
        def _(dve):
            done = [0]

            def link(ins):
                done[0] += 1
                ins.then_inc(setup_step, 1)
                dve.wait_ge(setup_step, done[0])

            nc.vector.memset(warm[:, 0:1], 1.0).then_inc(warm_set, 1)
            nc.vector.memset(tmp[:, 0:1], 0.0).then_inc(lo_ready, 2)
            nc.vector.memset(tmp[:, 1:2], 0.0).then_inc(y_ready, 2)
            nc.vector.memset(tmp[:, 2:3], 0.0).then_inc(transposed, 3)
            link(nc.vector.memset(triple[:, 0:1], 1.0))

            def statistics(g, s):
                if type(g) is int and g == 0:
                    if s * STAT % (CHUNK * PIX) == 0:
                        for q in range(Q):
                            dve.wait_ge(x_loaded[q], 16 * (s * STAT // (CHUNK * PIX) + 1))
                elif type(g) is int and g == 1:
                    if s in (0, FIRST):
                        for q in range(Q):
                            dve.wait_ge(x_loaded[q], (NCH + 1 if s == 0 else NCH + 2) * 16)
                elif s == 0:
                    for q in range(Q):
                        dve.wait_ge(x_loaded[q], (g + NCH + 1) * 16)
                xg = xin[:, bass.ds(g % XRING, 1), :, :].rearrange("p a c n -> p (a c n)")
                return nc.vector.bn_stats(bns[:, s, :], xg[:, s * STAT:(s + 1) * STAT])

            for s in range(FIRST):
                statistics(0, s)

            dve.wait_ge(weights_loaded, 160)
            nc.vector.tensor_tensor(outer7[:, :, :, :], k7h[:, :, :].unsqueeze(3).to_broadcast([P, CB, 7, 7]),
                                    k7w[:, :, :].unsqueeze(2).to_broadcast([P, CB, 7, 7]), ALU.mult)
            link(nc.vector.tensor_tensor(outer5[:, :, :, :], k5h[:, :, :].unsqueeze(3).to_broadcast([P, CB, 5, 5]),
                                         k5w[:, :, :].unsqueeze(2).to_broadcast([P, CB, 5, 5]), ALU.mult))
            link(nc.vector.tensor_tensor(k77[:, :, 1:6, 2:5], k77[:, :, 1:6, 2:5], k53[:, :, :, :], ALU.add))
            link(nc.vector.tensor_tensor(k77[:, :, 2:5, 1:6], k77[:, :, 2:5, 1:6], k35[:, :, :, :], ALU.add))
            link(nc.vector.tensor_tensor(k77[:, :, :, :], k77[:, :, :, :], outer7[:, :, :, :], ALU.add))
            link(nc.vector.tensor_tensor(k77[:, :, 1:6, 1:6], k77[:, :, 1:6, 1:6], outer5[:, :, :, :], ALU.add))
            flat = k77[:, :, :, :].rearrange("p c a b -> p c (a b)")
            link(nc.vector.scalar_tensor_tensor(out=kabs[:, :, :], in0=flat, scalar=-1.0, in1=flat, op0=ALU.mult, op1=ALU.max))
            link(nc.vector.tensor_reduce(kmax[:, :], kabs[:, :, :], AX.X, ALU.max))

            def aggregate(g):
                dve.wait_ge(stat_step, N_STAT_STEPS * g + 1)
                nc.vector.memset(pace[:, :], 0.0)
                nc.vector.bn_aggr(triple[:, 1:3], bns[:, :, :].rearrange("p s v -> p (s v)")).then_inc(triple_ready, 1)

            ve, r0, u = tmp[:, 0:1], tmp[:, 1:2], tmp[:, 2:3]

            def variance(g):
                dve.wait_ge(quad_loaded, (g + 1) * 16)
                nc.vector.memset(pace[:, :], 0.0)
                nc.vector.bn_aggr(mv[:, :], quad[:, :, :].rearrange("p q v -> p (q v)")).then_inc(stat_step, 1)
                dve.wait_ge(stat_step, N_STAT_STEPS * g + 2)
                nc.vector.tensor_scalar(ve, mv[:, 1:2], EPS, None, ALU.add).then_inc(var_ready, 1)


            def inverse_root(g):
                dve.wait_ge(root_ready, g + 1)
                nc.vector.reciprocal(r0, root[:, :]).then_inc(stat_step, 1)

            def newton(g):
                step = N_STAT_STEPS * g + 2
                dve.wait_ge(stat_step, step + 1)
                nc.vector.scalar_tensor_tensor(out=u, in0=r0, scalar=ve, in1=r0, op0=ALU.mult, op1=ALU.mult).then_inc(stat_step, 1)
                dve.wait_ge(stat_step, step + 2)
                nc.vector.tensor_scalar(u, u, -0.5 * XSCALE, 1.5 * XSCALE, ALU.mult, ALU.add).then_inc(stat_step, 1)

            def scale_and_shift(g):
                step = N_STAT_STEPS * g + 2
                nrm = norm[:, bass.ds(g % 2, 1), :].rearrange("p a n -> p (a n)")
                dve.wait_ge(stat_step, step + 3)
                nc.vector.tensor_tensor(nrm[:, 0:1], r0, u, ALU.mult).then_inc(stat_step, 1)
                dve.wait_ge(stat_step, step + 4)
                nc.vector.scalar_tensor_tensor(out=nrm[:, 1:2], in0=mv[:, 0:1], scalar=-1.0, in1=nrm[:, 0:1],
                                               op0=ALU.mult, op1=ALU.mult).then_inc(norm_ready, 1)

            def low(n, slot):
                dve.wait_ge(hi_ready, n + 1)
                nc.vector.tensor_tensor(xT[:, slot, 1, :], tps[:, slot, 0:NT * P], xT[:, slot, 0, :],
                                        ALU.subtract).then_inc(lo_ready, 1)

            def halo_parts(n, i):
                slot = i % 2
                for below in (False, True):
                    if below or i not in POOL_COPIES:
                        dst, src = halo_copy(slot, 0, below)
                        nc.vector.tensor_copy(dst, src)
                dve.wait_ge(lo_ready, n + 3)
                for below in (False, True):
                    dst, src = halo_copy(slot, 1, below)
                    ins = nc.vector.tensor_copy(dst, src)
                ins.then_inc(halo_rest, 1)

            def edge_matrices(g, k):
                dve.wait_ge(band_loaded[k], (g + 1) * 32)
                if not (type(g) is int and g == 0):
                    dve.wait_ge(conv_done, (g - 1) * CG + (k + 1) * CHUNK + 2)
                ch = slice(k * CHUNK, (k + 1) * CHUNK)
                top = (PAD + ROWS) * OW
                for below, m0 in ((False, top), (True, 0)):
                    src_p, lo_p = HALO_AT[below, 1]
                    m = band[src_p:src_p + SEG, ch, :, m0:m0 + PAD * OW]
                    nc.vector.tensor_copy(edge[src_p:src_p + SEG, ch, :, int(below), :], m)
                    ins = nc.vector.tensor_copy(edge[lo_p:lo_p + SEG, ch, 0, int(below), :], m[:, :, 0, :])
                ins.then_inc(edge_ready, 1)

            for s in range(FIRST, NSTAT):
                last = statistics(0, s)
            last.then_inc(stat_step, 1)
            aggregate(0)

            link(nc.vector.tensor_scalar(kmax[:, :], kmax[:, :], 1e-30, None, ALU.max))
            link(nc.vector.reciprocal(krec[:, :], kmax[:, :]))
            link(nc.vector.tensor_scalar(krec[:, :], krec[:, :], KSCALE, None, ALU.mult))
            link(nc.vector.tensor_tensor(kabs[:, :, :], flat, krec[:, :].unsqueeze(2).to_broadcast([P, CB, 49]), ALU.mult))
            dve.wait_ge(strip_zeroed, 1)
            hi, lo = [strip[:, :, part, :].rearrange("p c (a b) -> p c a b", b=OW)[:, :, OR - TAPS:, OW - TAPS:]
                      for part in range(2)]
            scaled = kabs[:, :, :].rearrange("p c (a b) -> p c a b", b=TAPS)
            link(nc.vector.tensor_copy(hi, scaled))
            nc.vector.tensor_tensor(lo, scaled, hi, ALU.subtract).then_inc(strip_ready, 1)
            nc.vector.tensor_scalar(chcol[:, 0, :], kmax[:, :], 1.0 / (KSCALE * XSCALE), None, ALU.mult)
            link(nc.vector.tensor_tensor(bia[:, 0, :], bia[:, 0, :], bia[:, 1, :], ALU.add))
            nc.vector.tensor_tensor(chcol[:, 1, :], bia[:, 0, :], bia[:, 2, :], ALU.add).then_inc(chcol_ready, 1)

            variance(0)
            inverse_root(0)
            newton(0)
            scale_and_shift(0)
            dve.wait_ge(triple_ready, 1)
            for s in range(FIRST):
                statistics(1, s)
            dve.wait_ge(edge_zeroed, 1)
            edge_matrices(0, 0)
            low(0, 0)
            dve.wait_ge(halo_zeroed, 1)
            halo_parts(0, 0)

            def steps(g):
                first = type(g) is int and g == 0
                more = [not (type(g) is int and g + ahead >= GROUPS) for ahead in range(3)]
                for i in range(CG):
                    if i + 1 < CG or more[1]:
                        low(g * CG + i + 1, (i + 1) % 2)
                    if i == VAR_AT + 1 and more[1]:
                        inverse_root(g + 1)
                    if i + 1 < CG or more[1]:
                        halo_parts(g * CG + i + 1, (i + 1) % CG)
                    if i in MATS_AT and more[MATS_AT[i][0]]:
                        edge_matrices(g + MATS_AT[i][0], MATS_AT[i][1])
                    if i == VAR_AT and more[1]:
                        variance(g + 1)
                    if (1 if first else 0) <= i <= LATE and more[1]:
                        n = -(-(NSTAT - FIRST) // LATE) if first else PIECES[i]
                        start = (i - 1) * n + FIRST if first else N_EARLY + sum(PIECES[:i])
                        for s in range(start, min(start + n, NSTAT)):
                            last = statistics(g + 1, s)
                        if i == LATE:
                            last.then_inc(stat_step, 1)
                            dve.wait_ge(triple_saved, (g + 1) * 16)
                            aggregate(g + 1)
                    if i == VAR_AT + 1 and more[1]:
                        newton(g + 1)
                    if i == (FIRST_EARLY if first else EARLY) and more[2]:
                        dve.wait_ge(triple_ready, g + 2)
                    n = FIRST_PER_STEP if first else PIECES[i]
                    start = (i - FIRST_EARLY) * n if first else sum(PIECES[EARLY:i])
                    if i >= (FIRST_EARLY if first else EARLY) and more[2]:
                        for s in range(start, min(start + n, N_EARLY)):
                            statistics(g + 2, s)
                    if i == VAR_AT + 1 and more[1]:
                        scale_and_shift(g + 1)

            steps(0)
            with dve.Fori(1, GROUPS - 2) as g:
                steps(g)
            steps(GROUPS - 2)
            steps(GROUPS - 1)

        @block.tensor
        def _(pe):
            def transpose(n, xslot, slot):
                pe.wait_ge(xnorm_ready, n + 1)
                pe.wait_ge(lo_ready, n + 1)
                for t in range(NT):
                    last = nc.tensor.transpose(tps[:, slot, t * P:(t + 1) * P],
                                               xnorm[:, xslot, t * P:(t + 1) * P], ident[:, :])
                last.then_inc(transposed, 1)

            spans = []
            for t in range(NT):
                reach = W - (t + 1) * TW - PAD
                for half in range(2):
                    lo, hi = max(reach, half * HALF), min(reach + OW, (half + 1) * HALF)
                    if lo < hi:
                        spans.append((t, half, lo - half * HALF, hi - lo, lo - reach))

            def convolve(g, i):
                n = g * CG + i
                slot = i % 2
                pe.wait_ge(hi_ready, n + 1)
                pe.wait_ge(y_ready, n + 1)
                started = set()
                for xpart, kpart in ((0, 0), (0, 1), (1, 0)):
                    if xpart == 1:
                        pe.wait_ge(lo_ready, n + 3)
                    mat = band[:, i, kpart, :].rearrange("p (h w) -> p h w", w=OW)[:, PAD:PAD + ROWS, :]
                    for t, half, col, cols, off in spans:
                        dst = cps[:, slot, half, 0:ROWS * HALF].rearrange("p (h w) -> p h w", w=HALF)
                        nc.tensor.matmul(dst[:, :, col:col + cols], xT[:, slot, xpart, t * P:(t + 1) * P],
                                         mat[:, :, off:off + cols], start=half not in started, stop=False,
                                         skip_group_check=True)
                        started.add(half)
                if i in POOL_COPIES:
                    pe.wait_ge(halo_above, g * len(POOL_COPIES) + POOL_COPIES.index(i) + 1)
                pe.wait_ge(halo_rest, n + 1)
                for kpart in range(2):
                    mat = edge[:, i, kpart, :, :].rearrange("p e (h w) -> p e h w", w=OW)
                    for j, (t, half, col, cols, off) in enumerate(spans):
                        dst = cps[:, slot, half, col:col + cols]
                        dst = bass.AP(dst.tensor, dst.offset,
                                      [dst.ap[0], [(ROWS - PAD) * HALF, 2], [HALF, PAD], [1, cols]])
                        stop = kpart == 1 and not any(s[1] == half for s in spans[j + 1:])
                        last = nc.tensor.matmul(dst, halo[:, slot, t * P:(t + 1) * P], mat[:, :, :, off:off + cols],
                                                start=False, stop=stop, skip_group_check=True)
                last.then_inc(conv_done, 1)

            pe.wait_ge(ident_ready, 1)
            pe.wait_ge(transposed, 3)
            transpose(0, 0, 0)

            def steps(g, last_group):
                for i in range(CG):
                    n = g * CG + i
                    if i + 1 < CG or not last_group:
                        transpose(n + 1, (i + 1) % 3, (i + 1) % 2)
                    if i % CHUNK == 0:
                        pe.wait_ge(band_loaded[i // CHUNK], (g + 1) * 32)
                        pe.wait_ge(edge_ready, g * NCH + i // CHUNK + 1)
                    convolve(g, i)

            with pe.Fori(0, GROUPS - 1) as g:
                steps(g, False)
            steps(GROUPS - 1, True)


_INS = ['x', 'L0_conv_w77', 'L0_conv_b77', 'L0_conv_w53', 'L0_conv_b53', 'L0_conv_w35', 'L0_conv_b35',
        'L0_conv_w7w', 'L0_conv_w7h', 'L0_conv_w5w', 'L0_conv_w5h']


def kernel(**inputs):
    import numpy as _np
    import concourse.bacc as _bacc
    from concourse import mybir as _mybir
    from concourse.bass_utils import run_bass_kernel_spmd as _run

    nc = _bacc.Bacc("TRN2", target_bir_lowering=False, num_devices=1)
    arrays, args = {}, []
    for name in _INS:
        a = _np.asarray(inputs[name])
        if a.ndim == 4 and name != 'x':
            a = a[:, :, ::-1, ::-1]
        a = _np.ascontiguousarray(a)
        arrays[f"in_{name}_dram"] = a
        args.append(nc.dram_tensor(f"in_{name}_dram", a.shape, _mybir.dt.from_np(a.dtype), kind="ExternalInput").ap())
    shape = arrays["in_x_dram"].shape
    args.append(nc.dram_tensor("out_0_dram", shape, _mybir.dt.float32, kind="ExternalOutput").ap())
    bass_groupnorm_dwconv_kernel(nc, *args)
    r = _run(nc, [arrays], core_ids=[0])
    return r.results[0]["out_0_dram"]
```
